# Optimizing a Trainium2 kernel written in Bass

```python
import numpy as np
import jax
import jax.numpy as jnp

def _softmax(x, axis=-1):
    return jax.nn.softmax(x, axis=axis)

def _gelu(x):
    return jax.nn.gelu(x, approximate=True)

def _silu(x):
    return jax.nn.silu(x)

def _sigmoid(x):
    return jax.nn.sigmoid(x)

def _layernorm(x, axis=-1, eps=1e-05):
    m = jnp.mean(x, axis=axis, keepdims=True)
    v = jnp.var(x, axis=axis, keepdims=True)
    return (x - m) / jnp.sqrt(v + eps)

def _scatter_add(tgt, idx, src, axis=0):
    return tgt.at[idx].add(src)

def _segment_sum(src, seg, n):
    return jax.ops.segment_sum(src, seg, n)
kernel_name = 'mk_gnn_preln_d2_gnn_r16_0e59d2'

def setup_inputs(seed: int=0):
    np.random.seed(seed)
    _w = jnp.asarray

    def _rec_inputs():
        import jax
        import jax.numpy as jnp
        _gk = jax.random.key(seed)
        x = -0.0003713 + 1 * jax.random.normal(jax.random.fold_in(_gk, 1), (3125, 256), jnp.float32)
        _s = jax.random.randint(jax.random.fold_in(_gk, 2), (50000,), 0, 3125, jnp.int32)
        _d = jax.random.randint(jax.random.fold_in(_gk, 3), (50000,), 0, 3125, jnp.int32)
        _loop = jnp.arange(3125, dtype=jnp.int32)
        src = jnp.concatenate([_s, _d, _loop])
        dst = jnp.concatenate([_d, _s, _loop])
        _o = jnp.argsort(dst, stable=True)
        src = src[_o]
        dst = dst[_o]
        edge_type_8 = jax.random.randint(jax.random.fold_in(_gk, 13), (103125,), 0, 8, jnp.int32)
        return (x, src, dst, edge_type_8)
    x, src, dst, edge_type_8 = _rec_inputs()

    def _L0_gnn_setup():
        import jax, jax.numpy as jnp
        import numpy as np
        N_NODES = 3125
        N_EDGES = 50000
        N_REL = 8
        DIM = 256

        def _rgcn_layer(x, W, b, src, dst, edge_type, num_nodes):
            xt = jnp.einsum('ni,rio->rno', x, W)
            msg = jax.nn.relu(xt[edge_type, src] + b)
            return jax.ops.segment_sum(msg, dst, num_segments=num_nodes)
        key = jax.random.key(seed)
        ks = jax.random.split(key, 6)
        x = jax.random.normal(ks[0], (N_NODES, DIM), dtype=jnp.float32)
        limit = float(np.sqrt(6.0 / (DIM + DIM)))
        W0 = jax.random.uniform(ks[1], (N_REL, DIM, DIM), dtype=jnp.float32, minval=-limit, maxval=limit)
        W1 = jax.random.uniform(ks[2], (N_REL, DIM, DIM), dtype=jnp.float32, minval=-limit, maxval=limit)
        b0 = jnp.zeros((DIM,), dtype=jnp.float32)
        b1 = jnp.zeros((DIM,), dtype=jnp.float32)
        edge_index = jax.random.randint(ks[3], (2, N_EDGES), 0, N_NODES, dtype=jnp.int64)
        edge_type = jax.random.randint(ks[4], (N_EDGES,), 0, N_REL, dtype=jnp.int64)
        return {'x': x, 'W0': W0, 'b0': b0, 'W1': W1, 'b1': b1, 'edge_index': edge_index, 'edge_type': edge_type}
    _L0_gnn_all = _L0_gnn_setup()
    _L0_gnn_in = {k: v for k, v in _L0_gnn_all.items() if k in ('W0', 'b0', 'W1', 'b1')}
    del _L0_gnn_all

    def _L1_gnn_setup():
        import jax, jax.numpy as jnp
        import numpy as np
        N_NODES = 1250
        N_EDGES = 20000
        EMB = 256
        key = jax.random.key(seed)
        k_h, k_s, k_d, k_w1, k_w2, k_b1, k_b2 = jax.random.split(key, 7)
        h = jax.random.normal(k_h, (N_NODES, EMB), dtype=jnp.float32)
        src = jax.random.randint(k_s, (N_EDGES,), 0, N_NODES, dtype=jnp.int32)
        dst = jax.random.randint(k_d, (N_EDGES,), 0, N_NODES, dtype=jnp.int32)
        gain = float(np.sqrt(2.0))
        std = gain * float(np.sqrt(2.0 / (EMB + EMB)))
        W_nb = jax.random.normal(k_w1, (EMB, EMB), dtype=jnp.float32) * std
        W_self = jax.random.normal(k_w2, (EMB, EMB), dtype=jnp.float32) * std
        b_nb = jax.random.uniform(k_b1, (EMB,), dtype=jnp.float32, minval=-0.06, maxval=0.06)
        b_self = jax.random.uniform(k_b2, (EMB,), dtype=jnp.float32, minval=-0.06, maxval=0.06)
        return {'h': h, 'W_nb': W_nb, 'b_nb': b_nb, 'W_self': W_self, 'b_self': b_self, 'src': src, 'dst': dst}
    _L1_gnn_all = _L1_gnn_setup()
    _L1_gnn_in = {k: v for k, v in _L1_gnn_all.items() if k in ('W_nb', 'b_nb', 'W_self', 'b_self')}
    del _L1_gnn_all
    return {'x': x, 'src': src, 'dst': dst, 'edge_type_8': edge_type_8, 'L0_gnn_W0': _L0_gnn_in['W0'], 'L0_gnn_b0': _L0_gnn_in['b0'], 'L0_gnn_W1': _L0_gnn_in['W1'], 'L0_gnn_b1': _L0_gnn_in['b1'], 'L1_gnn_W_nb': _L1_gnn_in['W_nb'], 'L1_gnn_b_nb': _L1_gnn_in['b_nb'], 'L1_gnn_W_self': _L1_gnn_in['W_self'], 'L1_gnn_b_self': _L1_gnn_in['b_self']}

def reference(x, src, dst, edge_type_8, L0_gnn_W0, L0_gnn_b0, L0_gnn_W1, L0_gnn_b1, L1_gnn_W_nb, L1_gnn_b_nb, L1_gnn_W_self, L1_gnn_b_self):
    import jax
    import jax.numpy as jnp

    def _L0_gnn_ref(x, W0, b0, W1, b1, edge_index, edge_type):
        import jax, jax.numpy as jnp
        import numpy as np
        N_NODES = 3125
        N_EDGES = 50000
        N_REL = 8
        DIM = 256

        def _rgcn_layer(x, W, b, src, dst, edge_type, num_nodes):
            xt = jnp.einsum('ni,rio->rno', x, W)
            msg = jax.nn.relu(xt[edge_type, src] + b)
            return jax.ops.segment_sum(msg, dst, num_segments=num_nodes)
        src, dst = (edge_index[0], edge_index[1])
        h = _rgcn_layer(x, W0, b0, src, dst, edge_type, x.shape[0])
        h = _rgcn_layer(h, W1, b1, src, dst, edge_type, x.shape[0])
        return h

    def _L1_gnn_ref(h, W_nb, b_nb, W_self, b_self, src, dst):
        import jax, jax.numpy as jnp
        import numpy as np
        N_NODES = 1250
        N_EDGES = 20000
        EMB = 256
        n = h.shape[0]
        neib_h = h @ W_nb.T + b_nb
        self_h = h @ W_self.T + b_self
        msg = self_h[src] + neib_h[dst]
        seg_max = jax.ops.segment_max(msg, dst, num_segments=n)
        e = jnp.exp(msg - seg_max[dst])
        seg_sum = jax.ops.segment_sum(e, dst, num_segments=n)
        alpha = e / seg_sum[dst]
        h_agg = jax.ops.segment_sum(alpha * h[src], dst, num_segments=n)
        deg = jax.ops.segment_sum(jnp.ones_like(dst, dtype=jnp.float32), dst, num_segments=n)
        return jnp.where((deg > 0)[:, None], h_agg, h)
    edge_index = jnp.stack([src, dst])
    h = jnp.maximum(_layernorm(x, axis=-1), 0.0)
    x = x + _L0_gnn_ref(h, L0_gnn_W0, L0_gnn_b0, L0_gnn_W1, L0_gnn_b1, edge_index, edge_type_8)
    h = jnp.maximum(_layernorm(x, axis=-1), 0.0)
    x = x + _L1_gnn_ref(h, L1_gnn_W_nb, L1_gnn_b_nb, L1_gnn_W_self, L1_gnn_b_self, src, dst)
    return x

_drawn_inputs = setup_inputs


def setup_inputs(seed=0):
    import zlib

    import numpy as np

    out = dict(_drawn_inputs(seed))
    spreads = {'L0_gnn_b0': (0.0, 0.1), 'L0_gnn_b1': (0.0, 0.719)}
    factors = {'L1_gnn_W_nb': 8.0, 'L1_gnn_b_nb': 8.0, 'L1_gnn_W_self': 8.0, 'L1_gnn_b_self': 8.0}
    for name, (base, spread) in spreads.items():
        noise = np.random.default_rng([zlib.crc32(name.encode()), seed]).standard_normal(out[name].shape)
        drawn = base * np.exp(spread * noise) if base else spread * noise
        out[name] = jnp.asarray(drawn.astype(out[name].dtype))
    for name, factor in factors.items():
        out[name] = (out[name] * factor).astype(out[name].dtype)
    return out
```

```python
from contextlib import ExitStack

import numpy as np
import concourse.bass as bass
from concourse import mybir

P = 128
WIN = 16
HALF = 13
SLOTS = 16
LEAD = 8
WINS = 64
KEY_BASE = 4096
PAD_DST = KEY_BASE - 1
LOWEST = -3.0e38
EPS = 1e-5


class Shapes:

    def __init__(self, n, d, r, e):
        self.N, self.D, self.R, self.E = n, d, r, e
        self.NT = -(-n // P)
        self.NP = self.NT * P
        self.TAIL = n - (self.NT - 1) * P
        self.ITERS = -(-e // (P * 2 * HALF))
        self.C = self.ITERS * 2 * HALF
        self.CG = -(-(self.C + 1) // P)
        self.CP = self.CG * P
        self.EP = self.CP * P
        self.K = d // P
        assert d == 2 * P and n < PAD_DST and r * d % 512 == 0


def gnn_kernel(nc, s, x, src, dst, etype, W0, b0, W1, b1, W_nb, b_nb, W_self, b_self, out):
    f32, bf16, i32, u32 = mybir.dt.float32, mybir.dt.bfloat16, mybir.dt.int32, mybir.dt.uint32
    ALU, ACTF, AX = mybir.AluOpType, mybir.ActivationFunctionType, mybir.AxisListType.X
    N, D, R, E, NT, NP, TAIL, C, CG, CP, K = s.N, s.D, s.R, s.E, s.NT, s.NP, s.TAIL, s.C, s.CG, s.CP, s.K
    ITERS, RD, G = s.ITERS, s.R * s.D, s.R * s.D // 512
    HALVES = 2 * ITERS
    ACCW = NP + WIN

    def dram(name, shape, dt):
        return nc.dram_tensor(name, shape, dt).ap()

    msg_table = [dram(f"msg_table{i}", (N * R + 1, D), f32) for i in range(2)]
    self_h_table = dram("self_h_table", (N + 1, 2 * D), f32)
    node_table = dram("node_table", (NP, 2 * D), f32)
    chunk_first_d = dram("chunk_first_d", (CP,), i32)
    chunk_last_d = dram("chunk_last_d", (CP,), f32)
    start_d = dram("start_d", (NP + 1,), f32)
    key_d = dram("key_d", (NP,), f32)
    ranked_d = dram("ranked_d", (NP, 4), i32)
    tiles_d = dram("tiles_d", (NT * 4,), i32)

    ctx = ExitStack()
    with ctx:
        def sb(name, shape, dt):
            return ctx.enter_context(nc.sbuf_tensor(name, shape, dt))

        def sem(name):
            return ctx.enter_context(nc.semaphore(name))

        ident = sb("ident", [P, P], f32)
        iota = sb("iota", [P, WINS], f32)
        node = sb("node", [P, NT], f32)
        node_key = sb("node_key", [P, NT], f32)
        before = sb("before", [NT, NT], f32)
        eps_col = sb("eps_col", [P, 1], f32)
        zeros = sb("zeros", [P, 2 * D], f32)
        no_edge = sb("no_edge", [1, 2 * D], f32)
        end_edge = sb("end_edge", [1, 1], f32)
        ones3 = sb("ones3", [3, P], bf16)

        first_c = sb("first_c", [P, CG], f32)
        first_ci = sb("first_ci", [P, CG], i32)
        last_c = sb("last_c", [P, CG], f32)
        row_cols = sb("row_cols", [P, CP], i32)
        local_cols = sb("local_cols", [P, CP], f32)
        chunk_first = sb("chunk_first", [1, CP], i32)
        last_all = sb("last_all", [P, CP], f32)
        chunks_below = sb("chunks_below", [P, NT], f32)
        chunks_below_i = sb("chunks_below_i", [P, NT], i32)
        edges_below = sb("edges_below", [P, NT], f32)
        start = sb("start", [P, NT], f32)
        start_next = sb("start_next", [P, NT], f32)
        deg = sb("deg", [P, NT], f32)
        key = sb("key", [P, NT], f32)
        rank = sb("rank", [P, NT], f32)
        rank_i = sb("rank_i", [P, NT], i32)
        to_rank = sb("to_rank", [P, NT, 4], i32)
        ranked = sb("ranked", [P, NT, 4], i32)
        rank_node = sb("rank_node", [P, NT], i32)
        rank_start = sb("rank_start", [P, NT], i32)
        rank_deg = sb("rank_deg", [P, NT], f32)
        slot_src = sb("slot_src", [P, NT, WINS], i32)
        tile_f = sb("tile_f", [NT, 1], f32)
        tile_tab = sb("tile_tab", [NT, 4], i32)
        tile_row = sb("tile_row", [1, NT * 4], i32)
        start_nat = sb("start_nat", [P, 2, NT], f32)
        no_in = sb("no_in", [P, NT], f32)

        stats = sb("stats", [P, NT, 6], f32)
        mean_var = sb("mean_var", [P, NT, 2], f32)
        rstd = sb("rstd", [P, NT], f32)
        shift = sb("shift", [P, NT], f32)
        h_tile = sb("h_tile", [P, 2, D], f32)
        hT = sb("hT", [P, 2, K, P], f32)

        bias_row = sb("bias_row", [1, 2, D], f32)
        bias_rest = sb("bias_rest", [1, 2, D], f32)
        bias_parts = sb("bias_parts", [1, 3, 2, D], bf16)
        bias3 = sb("bias3", [3, 2, D], bf16)
        w_att_n = sb("w_att_n", [P, 2, K, D], f32)
        w_att = sb("w_att", [P, K, 2, D], f32)
        b_att = sb("b_att", [P, 2, D], f32)

        row_stage = sb("row_stage", [P, 2, HALF], i32)
        onehot = sb("onehot", [P, 2, HALF, WIN], f32)
        slot_stage = sb("slot_stage", [P, 2, SLOTS], i32)

        acc1 = sb("acc1", [P, K, ACCW], f32)
        RING, W_W, OUT_W, ACC_W = 2 * HALF * D, K * RD, 2 * RD, K * ACCW
        AT_RING = 2 * SLOTS * 2 * D
        PREP_W = 6 * CP
        region = sb("region", [P, max(RING + 2 * W_W + OUT_W + max(ACC_W, PREP_W) + NP, AT_RING + NT * 2 * D)], f32)
        assert NT * D <= RING
        at = 0

        def view(words):
            nonlocal at
            at += words
            return region[:, at - words:at]

        ring = view(RING).rearrange("p (h j d) -> p h j d", h=2, d=D)
        x_all = region[:, 0:NT * D].rearrange("p (t d) -> p t d", d=D)
        weights = [view(W_W).rearrange("p (k n) -> p k n", k=K) for _ in range(2)]
        msg_out = view(OUT_W).rearrange("p (b n) -> p b n", b=2)
        acc0 = view(ACC_W).rearrange("p (k n) -> p k n", k=K)
        acc = [acc0, acc1]
        at -= ACC_W
        src_n, etype_n, dst_n = (view(CP).bitcast(i32).rearrange("p (g e) -> p g e", e=P) for _ in range(3))
        row_n, dstf_n, local_n = (view(CP).rearrange("p (g e) -> p g e", e=P) for _ in range(3))
        at += max(0, ACC_W - PREP_W)
        dst_rows = view(NP).bitcast(i32).rearrange("p (t e) -> p t e", e=P)
        at = 0
        at_ring = view(AT_RING).rearrange("p (b j c) -> p b j c", b=2, j=SLOTS)
        ranked_node = view(NT * 2 * D).rearrange("p (t c) -> p t c", t=NT)
        flat1 = acc1[:, :, :].rearrange("p k n -> p (k n)")
        key_all, scratch = flat1[:, 0:NP], flat1[:, NP:2 * NP]
        slot_valid, slot_srcf = (flat1[:, i * NT * WINS:(i + 1) * NT * WINS].rearrange("p (t j) -> p t j", j=WINS) for i in range(2))
        sh_out = msg_out[:, :, 0:2 * D]
        nb_out = msg_out[:, :, 2 * D:4 * D]

        run_max = sb("run_max", [P, D], f32)
        part_max = sb("part_max", [P, D], f32)
        msg_max = sb("msg_max", [P, 2, D], f32)
        logit_bias = sb("logit_bias", [P, D], f32)
        rescale = sb("rescale", [P, 2, D], f32)
        sums = sb("sums", [P, 2, D], f32)
        inv_sum = sb("inv_sum", [P, D], f32)

        psum = ctx.enter_context(nc.psum_tensor("psum", [P, 8, 512], f32))
        bank = [psum[:, i, :] for i in range(8)]
        ps_mm, ps_T, ps_prod, ps_prep = bank[0:4], (bank[4], bank[7]), bank[5:7], bank[7]
        at_psum = psum[:, 0:2, :]

        def sems(names):
            for n in names.split():
                yield sem(n)

        (x_loaded, x_cleared, edges_loaded, weights_loaded, bias_loaded, bias3_loaded, att_w_loaded, consts_made,
         edge_rows_stored, acc_cleared) = sems(
            "x_loaded x_cleared edges_loaded weights_loaded bias_loaded bias3_loaded att_w_loaded consts_made "
            "edge_rows_stored acc_cleared")
        (bias_split, rows_made, bounds_made, bounds_stored, bounds_loaded, cols_transposed, cols_copied, below_made,
         dst_rows_loaded, start_made, start_stored, start_next_loaded, start_nat_loaded, key_made, key_stored,
         key_loaded, rank_made, ranked_stored, ranked_loaded, rank_cols_made, slot_src_loaded, slots_masked,
         deg_transposed, tiles_made, tile_prefix, tile_tab_made, tile_tab_stored, tile_row_loaded, att_w_transposed,
         att_w_made) = sems(
            "bias_split rows_made bounds_made bounds_stored bounds_loaded cols_transposed cols_copied below_made "
            "dst_rows_loaded start_made start_stored start_next_loaded start_nat_loaded key_made key_stored "
            "key_loaded rank_made ranked_stored ranked_loaded rank_cols_made slot_src_loaded slots_masked "
            "deg_transposed tiles_made tile_prefix tile_tab_made tile_tab_stored tile_row_loaded att_w_transposed "
            "att_w_made")
        (stats_made, std_made, norm_made, h_made, h_transposed, hT_made, mm_done, evacuated) = sems(
            "stats_made std_made norm_made h_made h_transposed hT_made mm_done evacuated")
        (stage_ready, onehot_ready, half_multiplied, half_added) = sems(
            "stage_ready onehot_ready half_multiplied half_added")
        (acc_copied, acc_transposed, x_added, node_mm_done, node_out_made) = sems(
            "acc_copied acc_transposed x_added node_mm_done node_out_made")
        (ranked_node_loaded, scale_ready, lead_ready, rest_ready, scale_exp, lead_exp, rest_exp, lead_weighted,
         rest_weighted, lead_summed, rest_summed, block_folded, tile_done, out_stored) = sems(
            "ranked_node_loaded scale_ready lead_ready rest_ready scale_exp lead_exp rest_exp lead_weighted "
            "rest_weighted lead_summed rest_summed block_folded tile_done out_stored")
        passed = sem("passed")
        msg_stored = [sem(f"msg_stored{b}") for b in range(2)]
        node_stored = [sem(f"node_stored{b}") for b in range(2)]
        rows_landed = [sem(f"rows_landed{b}") for b in range(2)]
        slots_staged = [sem(f"slots_staged{b}") for b in range(2)]
        lead_landed = [sem(f"lead_landed{b}") for b in range(2)]
        rest_landed = [sem(f"rest_landed{b}") for b in range(2)]

        def credits(eng):
            for one in (half_multiplied, half_added, h_transposed, hT_made, acc_transposed, x_added, node_mm_done,
                        node_out_made, scale_ready, lead_summed, rest_summed, block_folded):
                eng.sem_inc(one, 2)
            eng.sem_inc(mm_done, 2 * G)
            eng.sem_inc(evacuated, G)
            for b in range(2):
                eng.sem_inc(msg_stored[b], 16)
                eng.sem_inc(node_stored[b], 32)

        ctx.enter_context(nc.allow_non_contiguous_dma("small index tables"))
        block = ctx.enter_context(nc.Block())

        def rows_at(col):
            return bass.IndirectOffsetOnAxis(ap=col.bitcast(u32), axis=0)

        def flat(ap):
            return ap.rearrange("p a d -> p (a d)")

        def tile_rows(t):
            return TAIL if isinstance(t, int) and t == NT - 1 else P

        def node_tiles(eng, step):
            with eng.Fori(0, NT // 2) as i:
                step(2 * i, 0)
                step(2 * i + 1, 1)
            for t in range(NT // 2 * 2, NT):
                step(t, t % 2)

        def node_tiles_ahead(eng, ahead, step):
            assert NT % 2
            ahead(0, 0)
            with eng.Fori(0, NT // 2) as i:
                ahead(2 * i + 1, 1)
                step(2 * i, 0)
                ahead(2 * i + 2, 0)
                step(2 * i + 1, 1)
            step(NT - 1, 0)

        MAX_BLOCKS = CP * P // SLOTS + NT

        def attention_blocks(eng, at_tile, at_block):
            with eng.Fori(0, NT) as t:
                def entry(w, least, most):
                    return eng.value_load(tile_row[0:1, bass.ds(4 * t + w, 1)], min_val=least, max_val=most)
                blocks, quads, base = entry(0, 1, MAX_BLOCKS), entry(1, 2, 4 * MAX_BLOCKS), entry(2, 0, MAX_BLOCKS)
                at_tile(t)
                with eng.Fori(0, blocks) as j:
                    at_block(t, j, eng.snap(base + j), eng.snap(quads - 4 * j))

        def rest_of_block(eng, left, eight, four, none):
            with eng.If(left > 3):
                eight()
            with eng.Else():
                with eng.If(left > 2):
                    four()
                with eng.Else():
                    none()

        @block.sync
        def _(sp):
            def load_x(turn):
                sp.wait_ge(x_cleared, turn + 1)
                for t in range(NT):
                    sp.dma_start(x_all[0:tile_rows(t), t, :], x[t * P:min(N, (t + 1) * P), :]).then_inc(x_loaded, 16)

            load_x(0)
            for a, tile in ((src, src_n), (etype, etype_n), (dst, dst_n)):
                sp.dma_start(tile, a.rearrange("(g p e) -> p g e", p=P, e=P)).then_inc(edges_loaded, 16)
            for i, b in enumerate((b0, b1)):
                sp.dma_start(bias_row[0:1, i, :], b.rearrange("(o d) -> o d", o=1)).then_inc(bias_loaded, 16)
            for i, w in enumerate((W0, W1)):
                for k in range(K):
                    sp.dma_start(weights[i][:, k, :].rearrange("p (r o) -> p r o", r=R),
                                 w[:, k * P:(k + 1) * P, :].rearrange("r i o -> i r o")).then_inc(weights_loaded, 16)
            for i, (w, b) in enumerate(((W_self, b_self), (W_nb, b_nb))):
                sp.dma_start(w_att_n[:, i, :, :], w.rearrange("(k p) i -> p k i", p=P)).then_inc(att_w_loaded, 16)
                sp.dma_start(b_att[:, i, :], b.rearrange("(o d) -> o d", o=1).broadcast_to([P, D])).then_inc(att_w_loaded, 16)
            sp.wait_ge(consts_made, 1)
            for table in msg_table:
                sp.dma_start(table[N * R:N * R + 1, :], zeros[0:1, 0:D]).then_inc(edge_rows_stored, 16)
            sp.dma_start(self_h_table[N:N + 1, :], no_edge[0:1, :]).then_inc(edge_rows_stored, 16)
            
            sp.wait_ge(bias_split, 1)
            for i in range(3):
                sp.dma_start(bias3[i:i + 1, :, :], bias_parts[0:1, i, :, :]).then_inc(bias3_loaded, 16)
            for layer in range(2):
                def store(t, b):
                    n = tile_rows(t)
                    sp.wait_ge(evacuated, G * (layer * NT + t + 2))
                    sp.dma_start(msg_table[layer][0:N * R, :].rearrange("(n r) d -> n (r d)", r=R)[bass.ds(t * P, n), :],
                                 msg_out[0:n, b, :]).then_inc(msg_stored[b], 16)
                node_tiles(sp, store)
                if layer == 0:
                    sp.wait_ge(tile_tab_made, 1)
                    sp.dma_start(tiles_d.rearrange("(t w) -> t w", w=4), tile_tab[:]).then_inc(tile_tab_stored, 16)
                    sp.wait_ge(tile_tab_stored, 16)
                    sp.dma_start(tile_row[:], tiles_d.rearrange("(o w) -> o w", o=1)).then_inc(tile_row_loaded, 16)

            load_x(1)

            def store_node(t, b):
                n = tile_rows(t)
                sp.wait_ge(node_out_made, t + 3)
                sp.dma_start(self_h_table[bass.ds(t * P, n), :], sh_out[0:n, b, :]).then_inc(node_stored[b], 16)
                sp.dma_start(node_table[bass.ds(t * P, P), :], nb_out[:, b, :]).then_inc(node_stored[b], 16)
            node_tiles(sp, store_node)

            sp.wait_ge(slots_masked, 1)
            sp.wait_ge(tile_row_loaded, 16)

            def stage(t, j, k, left):
                sp.wait_ge(scale_ready, k + 1)
                sp.sem_inc(passed, 1)

                def load(b):
                    listed = nc.s_assert_within(j, 0, WINS // SLOTS - 1,
                                                skip_runtime_bounds_check_because="the branch is for the listed blocks only")
                    sp.dma_start(slot_stage[:, b, :], flat(slot_src[:, bass.ds(t, 1), bass.ds(listed * SLOTS, SLOTS)])).then_inc(slots_staged[b], 16)
                with sp.If(j < WINS // SLOTS):
                    with sp.If(k % 2 < 1):
                        load(0)
                    with sp.Else():
                        load(1)
            attention_blocks(sp, lambda t: None, stage)
            sp.wait_ge(out_stored, 16 * NT)

        @block.gpsimd
        def _(pool):
            g = nc.gpsimd
            g.memset(x_all[:, NT - 1, :], 0.0).then_inc(x_cleared, 1)
            g.memset(zeros[:], 0.0)
            g.memset(no_edge[0:1, 0:D], LOWEST)
            g.memset(no_edge[0:1, D:2 * D], 0.0)
            g.memset(end_edge[:], float(E))
            g.memset(ones3[:], 1.0)
            g.memset(eps_col[:], EPS)
            g.memset(before[:], 1.0)
            g.memset(ident[:], 0.0)
            g.iota(iota[:], pattern=[[1, WINS]], base=0, channel_multiplier=0, allow_small_or_imprecise_dtypes=True)
            g.iota(node[:], pattern=[[1, NT]], base=0, channel_multiplier=NT, allow_small_or_imprecise_dtypes=True)
            g.iota(node_key[:], pattern=[[-1, NT]], base=KEY_BASE - 1, channel_multiplier=-NT, allow_small_or_imprecise_dtypes=True)
            pool.drain()
            g.affine_select(out=ident[:], in_=ident[:], compare_op=ALU.not_equal, fill=1.0, base=0, pattern=[[-1, P]], channel_multiplier=1)
            g.affine_select(out=before[:], in_=before[:], compare_op=ALU.is_gt, fill=0.0, base=0, pattern=[[1, NT]], channel_multiplier=-1)
            pool.drain().then_inc(consts_made, 1)
            g.memset(sums[:], 0.0)

            pool.wait_ge(bounds_made, 1)
            pool.dma_start(chunk_first_d.rearrange("(g p) -> p g", p=P), first_ci[:]).then_inc(bounds_stored, 16)
            pool.dma_start(chunk_last_d.rearrange("(g p) -> p g", p=P), last_c[:]).then_inc(bounds_stored, 16)
            pool.wait_ge(bounds_stored, 32)
            pool.dma_start(chunk_first[:], chunk_first_d.rearrange("(o c) -> o c", o=1)).then_inc(bounds_loaded, 16)
            pool.dma_start(last_all[:], chunk_last_d.rearrange("(o c) -> o c", o=1).broadcast_to([P, CP])).then_inc(bounds_loaded, 16)

            pool.wait_ge(below_made, 1)
            for t in range(NT):
                pool.indirect_dma_start(out=dst_rows[:, t, :], out_offset=None, in_=dst.rearrange("(c e) -> c e", e=P),
                                        in_offset=rows_at(chunks_below_i[:, t:t + 1])).then_inc(dst_rows_loaded, 16)
            pool.wait_ge(cols_copied, 2 * CG)
            g.memset(acc0, 0.0).then_inc(acc_cleared, 1)
            pool.dma_start(start_d[NP:NP + 1].rearrange("(o d) -> o d", o=1), end_edge[0:1, 0:1]).then_inc(start_stored, 16)
            pool.wait_ge(start_made, 1)
            pool.dma_start(start_d[0:NP].rearrange("(p t) -> p t", p=P), start[:]).then_inc(start_stored, 16)
            pool.wait_ge(start_stored, 32)
            pool.dma_start(start_next[:], start_d[1:NP + 1].rearrange("(p t) -> p t", p=P)).then_inc(start_next_loaded, 16)
            for i in range(2):
                pool.dma_start(start_nat[:, i, :], start_d[i:NP + i].rearrange("(t p) -> p t", p=P)).then_inc(start_nat_loaded, 16)
            pool.wait_ge(key_made, 1)
            pool.dma_start(key_d.rearrange("(p t) -> p t", p=P), key[:]).then_inc(key_stored, 16)
            pool.wait_ge(key_stored, 16)
            pool.dma_start(key_all, key_d.rearrange("(o n) -> o n", o=1).broadcast_to([P, NP])).then_inc(key_loaded, 16)
            pool.wait_ge(rank_made, 1)
            for t in range(NT):
                pool.indirect_dma_start(out=ranked_d, out_offset=rows_at(rank_i[:, t:t + 1]), in_=to_rank[:, t, :],
                                        in_offset=None).then_inc(ranked_stored, 16)
            pool.wait_ge(ranked_stored, 16 * NT)
            pool.dma_start(ranked[:], ranked_d.rearrange("(t p) w -> p t w", p=P)).then_inc(ranked_loaded, 16)
            pool.wait_ge(rank_cols_made, 1)
            for t in range(NT):
                pool.indirect_dma_start(out=slot_src[:, t, :], out_offset=None, in_=src.rearrange("(e o) -> e o", o=1),
                                        in_offset=rows_at(rank_start[:, t:t + 1])).then_inc(slot_src_loaded, 16)

            pool.wait_ge(edge_rows_stored, 48)
            for layer in range(2):
                for b in range(2):
                    pool.wait_ge(msg_stored[b], 16 * (1 + (layer + 1) * len(range(b, NT, 2))))
                with pool.Fori(0, ITERS) as i:
                    for half in range(2):
                        pool.wait_ge(stage_ready, layer * HALVES + 2 * i + half + 1)
                        pool.sem_inc(passed, 1)
                        for j in range(HALF):
                            pool.indirect_dma_start(out=ring[:, half, j, :], out_offset=None, in_=msg_table[layer],
                                                    in_offset=rows_at(row_stage[:, half, j:j + 1])).then_inc(rows_landed[half], 16)

            pool.wait_ge(half_added, 2 * HALVES + 2)
            g.memset(x_all[:, NT - 1, :], 0.0).then_inc(x_cleared, 1)

            for b in range(2):
                pool.wait_ge(node_stored[b], 32 * (1 + len(range(b, NT, 2))))
            for t in range(NT):
                pool.indirect_dma_start(out=ranked_node[:, t, :], out_offset=None, in_=node_table,
                                        in_offset=rows_at(rank_node[:, t:t + 1])).then_inc(ranked_node_loaded, 16)
            pool.wait_ge(tile_row_loaded, 16)

            def gather_block(t, j, k, left):
                def gather(b, first, last, landed):
                    for slot in range(first, last):
                        pool.indirect_dma_start(out=at_ring[:, b, slot, :], out_offset=None, in_=self_h_table,
                                                in_offset=rows_at(slot_stage[:, b, slot:slot + 1])).then_inc(landed, 16)

                def into(b):
                    pool.wait_ge(slots_staged[b], 16 * (k // 2) + 16)
                    pool.wait_ge(lead_summed, k + 1)
                    pool.sem_inc(passed, 1)
                    gather(b, 0, LEAD, lead_landed[b])
                    pool.wait_ge(rest_summed, k + 1)
                    pool.sem_inc(passed, 1)
                    rest_of_block(pool, left, lambda: gather(b, LEAD, SLOTS, rest_landed[b]), lambda: gather(b, LEAD, LEAD + 4, rest_landed[b]), lambda: None)
                with pool.If(k % 2 < 1):
                    into(0)
                with pool.Else():
                    into(1)
            attention_blocks(pool, lambda t: None, gather_block)
            pool.wait_ge(tile_done, NT)
            for t in range(NT):
                n = tile_rows(t)
                pool.indirect_dma_start(out=out, out_offset=rows_at(rank_node[0:n, t:t + 1]), in_=ranked_node[0:n, t, D:2 * D],
                                        in_offset=None).then_inc(out_stored, 16)

        @block.scalar
        def _(act):
            a = nc.scalar
            credits(act)

            for i in range(2 * CG):
                act.wait_ge(cols_transposed, i + 1)
                a.copy((row_cols, local_cols)[i % 2][:, i // 2 * P:(i // 2 + 1) * P], bank[i % 4][:, 0:P]).then_inc(cols_copied, 1)

            def std(turn):
                act.wait_ge(stats_made, turn + 1)
                a.activation(rstd[:], mean_var[:, :, 1], ACTF.Sqrt, bias=eps_col[:]).then_inc(std_made, 1)
                act.wait_ge(norm_made, turn + 1)

            def relu_norm(t, b, n):
                act.wait_ge(h_transposed, n + 1)
                a.activation(h_tile[:, b, :], flat(x_all[:, bass.ds(t, 1), :]), ACTF.Relu,
                             bias=shift[:, bass.ds(t, 1)], scale=rstd[:, bass.ds(t, 1)]).then_inc(h_made, 1)

            def copy_hT(b, n):
                act.wait_ge(h_transposed, n + 3)
                a.copy(hT[:, b, :, :], ps_T[b][:, 0:D].rearrange("p (k n) -> p k n", k=K)).then_inc(hT_made, 1)

            def evacuate(t, b, layer):
                n = layer * NT + t
                act.wait_ge(msg_stored[b], 16 * (layer * len(range(b, NT, 2)) + t // 2 + 1))
                for gr in range(G):
                    act.wait_ge(mm_done, 2 * G + G * n + gr + 1)
                    a.activation(msg_out[:, b, gr * 512:(gr + 1) * 512], ps_mm[gr], ACTF.Relu).then_inc(evacuated, 1)

            std(0)

            def layer1_input(t, b):
                relu_norm(t, b, t)
                act.wait_ge(mm_done, G * (t + 1))
                copy_hT(b, t)
            node_tiles_ahead(act, layer1_input, lambda t, b: evacuate(t, b, 0))

            def stage_rows(layer):
                with act.Fori(0, ITERS) as i:
                    for half in range(2):
                        act.wait_ge(half_multiplied, layer * HALVES + 2 * i + half + 1)
                        a.copy(row_stage[:, half, :], row_cols[:, bass.ds((2 * i + half) * HALF, HALF)]).then_inc(stage_ready, 1)

            stage_rows(0)
            act.wait_ge(half_added, HALVES + 2)

            def layer2_input(t, b):
                act.wait_ge(mm_done, G * (NT + t + 1))
                a.copy(hT[:, b, :, :], acc[0][:, :, bass.ds(t * P, P)]).then_inc(hT_made, 1)
            node_tiles_ahead(act, layer2_input, lambda t, b: evacuate(t, b, 1))
            stage_rows(1)
            act.wait_ge(half_added, 2 * HALVES + 2)

            def turn_acc(t, b):
                act.wait_ge(acc_transposed, t + 1)
                a.copy(hT[:, b, :, :], acc[1][:, :, bass.ds(t * P, P)]).then_inc(acc_copied, 1)
            node_tiles(act, turn_acc)

            std(1)

            def node_input(t, b):
                act.wait_ge(node_out_made, t + 1)
                relu_norm(t, b, NT + t)
                act.wait_ge(node_mm_done, t + 1)
                copy_hT(b, NT + t)
            node_tiles(act, node_input)

            act.wait_ge(tile_row_loaded, 16)

            def exponentials(t, j, k, left):
                buf = act.snap(k % 2)

                def exp(first, last):
                    w = at_ring[:, bass.ds(buf, 1), first:last, 0:D].rearrange("p b j c -> p (b j) c")
                    return a.activation(w, w, ACTF.Exp)
                act.wait_ge(scale_ready, k + 3)
                w = flat(rescale[:, bass.ds(buf, 1), :])
                a.activation(w, w, ACTF.Exp).then_inc(scale_exp, 1)
                act.wait_ge(lead_ready, k + 1)
                exp(0, LEAD).then_inc(lead_exp, 1)
                act.wait_ge(rest_ready, k + 1)
                act.sem_inc(passed, 1)
                rest_of_block(act, left, lambda: exp(LEAD, SLOTS).then_inc(rest_exp, 1),
                              lambda: exp(LEAD, LEAD + 4).then_inc(rest_exp, 1), lambda: act.drain().then_inc(rest_exp, 1))
            attention_blocks(act, lambda t: None, exponentials)

        @block.vector
        def _(dve):
            v = nc.vector

            def then(*_):
                dve.drain()

            def tile_stats(t):
                v.bn_stats(flat(stats[:, bass.ds(t, 1), :]), flat(x_all[:, bass.ds(t, 1), :]))

            def finish_norm(turn):
                dve.drain()
                for t in range(NT):
                    v.bn_aggr(mean_var[:, t, :], stats[:, t, :])
                dve.drain().then_inc(stats_made, 1)
                dve.wait_ge(std_made, turn + 1)
                then(v.reciprocal(rstd[:], rstd[:]))
                v.scalar_tensor_tensor(shift[:], mean_var[:, :, 0], -1.0, rstd[:], ALU.mult, ALU.mult).then_inc(norm_made, 1)

            dve.wait_ge(bias_loaded, 32)
            then(v.tensor_copy(bias_parts[0:1, 0, :, :], bias_row[:]))
            then(v.tensor_tensor(bias_rest[:], bias_row[:], bias_parts[0:1, 0, :, :], ALU.subtract))
            then(v.tensor_copy(bias_parts[0:1, 1, :, :], bias_rest[:]))
            then(v.tensor_tensor(bias_rest[:], bias_rest[:], bias_parts[0:1, 1, :, :], ALU.subtract))
            v.tensor_copy(bias_parts[0:1, 2, :, :], bias_rest[:]).then_inc(bias_split, 1)

            dve.wait_ge(edges_loaded, 48)
            v.scalar_tensor_tensor(row_n, src_n, float(R), etype_n, ALU.mult, ALU.add)
            then(v.tensor_copy(dstf_n, dst_n))
            v.tensor_reduce(last_c[:], dstf_n, AX, ALU.max)
            then(v.tensor_reduce(first_c[:], dstf_n, AX, ALU.min))
            then(v.tensor_scalar(first_c[:], first_c[:], float(NP), None, ALU.min))
            v.tensor_copy(first_ci[:], first_c[:])
            v.tensor_tensor(local_n, dstf_n, first_c[:, :, None].broadcast_to([P, CG, P]), ALU.subtract)
            dve.drain().then_inc(rows_made, 1)
            dve.nop().then_inc(bounds_made, 1)

            dve.wait_ge(x_loaded, 16 * NT)
            with dve.Fori(0, NT) as t:
                tile_stats(t)
            finish_norm(0)

            dve.wait_ge(consts_made, 1)
            dve.wait_ge(bounds_loaded, 32)
            for t in range(NT):
                then(v.tensor_scalar(scratch[:, 0:CP], last_all[:], node[:, t:t + 1], None, ALU.is_lt, ALU.add,
                                     accum_out=chunks_below[:, t:t + 1]))
            v.tensor_copy(chunks_below_i[:], chunks_below[:]).then_inc(below_made, 1)
            dve.wait_ge(dst_rows_loaded, 16 * NT)
            below = scratch.rearrange("p (t e) -> p t e", e=P)
            then(v.tensor_tensor(below, dst_rows, node[:, :, None].broadcast_to([P, NT, P]), ALU.is_lt))
            then(v.tensor_reduce(edges_below[:], below, AX, ALU.add))
            v.scalar_tensor_tensor(start[:], chunks_below[:], float(P), edges_below[:], ALU.mult, ALU.add).then_inc(start_made, 1)
            dve.wait_ge(start_next_loaded, 16)
            then(v.tensor_tensor(deg[:], start_next[:], start[:], ALU.subtract))
            then(v.tensor_scalar(key[:], deg[:], float(KEY_BASE - 1), float(KEY_BASE), ALU.min, ALU.mult))
            v.tensor_tensor(key[:], key[:], node_key[:], ALU.add).then_inc(key_made, 1)
            for w, col in enumerate((node, start, deg, node)):
                v.tensor_copy(to_rank[:, :, w], col[:])
            dve.wait_ge(start_nat_loaded, 32)
            v.tensor_tensor(no_in[:], start_nat[:, 1, :], start_nat[:, 0, :], ALU.is_equal)
            dve.wait_ge(key_loaded, 16)
            for t in range(NT):
                then(v.tensor_scalar(scratch, key_all, key[:, t:t + 1], None, ALU.is_gt, ALU.add, accum_out=rank[:, t:t + 1]))
            v.tensor_copy(rank_i[:], rank[:]).then_inc(rank_made, 1)
            dve.wait_ge(ranked_loaded, 16)
            v.tensor_copy(rank_node[:], ranked[:, :, 0])
            v.tensor_copy(rank_start[:], ranked[:, :, 1])
            v.tensor_copy(rank_deg[:], ranked[:, :, 2])
            dve.drain().then_inc(rank_cols_made, 1)
            v.tensor_tensor(slot_valid, iota[:, None, :].broadcast_to([P, NT, WINS]),
                            rank_deg[:, :, None].broadcast_to([P, NT, WINS]), ALU.is_lt)
            dve.wait_ge(slot_src_loaded, 16 * NT)
            then(v.tensor_scalar(slot_srcf, slot_src[:], float(-N), None, ALU.add))
            then(v.tensor_tensor(slot_srcf, slot_srcf, slot_valid, ALU.mult))
            v.tensor_scalar(slot_src[:], slot_srcf, float(N), None, ALU.add).then_inc(slots_masked, 1)
            blocks, quads, prefix, spare = (tile_tab[:, w:w + 1] for w in range(4))
            dve.wait_ge(deg_transposed, 1)
            then(v.tensor_reduce(tile_f[:], ps_prep[0:NT, 0:P], AX, ALU.max))
            then(v.tensor_scalar(spare, tile_f[:], 3.0, None, ALU.add))
            then(v.tensor_scalar(quads, spare, 2, None, ALU.arith_shift_right))
            then(v.tensor_scalar(quads, quads, 2.0, None, ALU.max))
            then(v.tensor_scalar(spare, quads, 3, None, ALU.bitwise_and))
            then(v.tensor_scalar(spare, spare, 1.0, None, ALU.is_equal))
            then(v.tensor_tensor(tile_f[:], quads, spare, ALU.add))
            v.tensor_copy(quads, tile_f[:])
            then(v.tensor_scalar(spare, tile_f[:], 3.0, None, ALU.add))
            then(v.tensor_scalar(blocks, spare, 2, None, ALU.arith_shift_right))
            v.tensor_copy(tile_f[:], blocks).then_inc(tiles_made, 1)
            dve.wait_ge(tile_prefix, 1)
            then(v.tensor_copy(prefix, ps_prep[0:NT, P:P + 1]))
            dve.wait_ge(att_w_transposed, 1)
            for i in range(2):
                for ko in range(K):
                    v.tensor_copy(w_att[:, :, i, ko * P:(ko + 1) * P], ps_mm[2 * i + ko][:, 0:D].rearrange("p (k o) -> p k o", k=K))
            v.memset(acc1[:], 0.0)
            dve.drain().then_inc(att_w_made, 1)
            dve.nop().then_inc(tile_tab_made, 1)

            def make_onehot(layer, i, half):
                h = layer * HALVES + 2 * i + half
                dve.wait_ge(half_multiplied, h + 1)
                cols = local_cols[:, bass.ds((2 * i + half) * HALF, HALF)]
                v.tensor_tensor(onehot[:, half, :, :], iota[:, None, 0:WIN].broadcast_to([P, HALF, WIN]),
                                cols[:, :, None].broadcast_to([P, HALF, WIN]), ALU.is_equal).then_inc(onehot_ready, 1)

            def add_half(layer, i, half):
                h = layer * HALVES + 2 * i + half
                dve.wait_ge(half_multiplied, h + 3)
                for j in range(HALF):
                    w = dve.value_load(chunk_first[0:1, bass.ds((2 * i + half) * HALF + j, 1)], min_val=0, max_val=NP)
                    a = acc[layer][:, :, bass.ds(w, WIN)]
                    p = ps_prod[half][:, j * K * WIN:(j + 1) * K * WIN].rearrange("p (k w) -> p k w", k=K)
                    add = v.tensor_tensor(a, a, p, ALU.add)
                    if j == HALF - 1:
                        add.then_inc(half_added, 1)
                    dve.drain()

            dve.wait_ge(cols_copied, 2 * CG)
            dve.wait_ge(acc_cleared, 1)
            for layer in range(2):
                make_onehot(layer, 0, 0)
                make_onehot(layer, 0, 1)
                with dve.Fori(0, ITERS - 1) as i:
                    for half in range(2):
                        add_half(layer, i, half)
                        make_onehot(layer, i + 1, half)
                for half in range(2):
                    add_half(layer, ITERS - 1, half)

            dve.wait_ge(x_loaded, 2 * 16 * NT)

            def add_x(t, b):
                dve.wait_ge(acc_transposed, t + 3)
                xt = flat(x_all[:, bass.ds(t, 1), :])
                then(v.tensor_tensor(xt, xt, ps_T[b][:, 0:D], ALU.add).then_inc(x_added, 1))
                tile_stats(t)
            node_tiles(dve, add_x)
            finish_norm(1)

            def node_out(t, b):
                dve.wait_ge(node_mm_done, t + 3)
                dve.wait_ge(node_stored[b], 32 * (t // 2 + 1))
                v.tensor_tensor(sh_out[:, b, 0:D], ps_mm[b][:, 0:D], b_att[:, 0, :], ALU.add)
                v.tensor_tensor(nb_out[:, b, 0:D], ps_mm[b][:, D:2 * D], b_att[:, 1, :], ALU.add)
                v.tensor_copy(sh_out[:, b, D:2 * D], h_tile[:, b, :])
                v.scalar_tensor_tensor(nb_out[:, b, D:2 * D], h_tile[:, b, :], no_in[:, bass.ds(t, 1)],
                                       flat(x_all[:, bass.ds(t, 1), :]), ALU.mult, ALU.add)
                dve.drain().then_inc(node_out_made, 1)
            node_tiles(dve, node_out)

            dve.wait_ge(ranked_node_loaded, 16 * NT)
            dve.wait_ge(tile_row_loaded, 16)

            landed = [dve.alloc_register(f"landed{b}") for b in range(2)]
            for one in landed:
                dve.reg_mov(one, 16 * 4)

            def fold_in(k, buf):
                dve.wait_ge(lead_summed, k + 2)
                dve.wait_ge(rest_summed, k + 2)
                dve.wait_ge(scale_exp, k)
                then(v.tensor_tensor(sums[:], sums[:], rescale[:, bass.ds(buf, 1), :].broadcast_to([P, 2, D]), ALU.mult))
                part = at_psum[:, bass.ds(buf, 1), :].rearrange("p b (s c) -> p (b s) c", s=2)
                then(v.tensor_tensor(sums[:], sums[:], part, ALU.add).then_inc(block_folded, 1))

            def finish_tile(t):
                then(v.reciprocal(inv_sum[:], sums[:, 0, :]))
                then(v.tensor_tensor(inv_sum[:], inv_sum[:], sums[:, 1, :], ALU.mult))
                res = flat(ranked_node[:, bass.ds(t, 1), D:2 * D])
                v.tensor_tensor(res, res, inv_sum[:], ALU.add).then_inc(tile_done, 1)

            def start_tile(t):
                v.memset(run_max[:], LOWEST)
                then(v.memset(msg_max[:], LOWEST))

            def softmax_block(t, j, k, left):
                buf, other = dve.snap(k % 2), dve.snap((k + 1) % 2)
                neib = flat(ranked_node[:, bass.ds(t, 1), 0:D])

                def slots(first, last, col):
                    return at_ring[:, bass.ds(buf, 1), first:last, col * D:(col + 1) * D].rearrange("p b j c -> p (b j) c")

                def fold_max(first, last):
                    then(v.tensor_reduce(part_max[:], slots(first, last, 0).rearrange("p j c -> p c j"), AX, ALU.max))
                    then(v.tensor_tensor(run_max[:], run_max[:], part_max[:], ALU.max))

                def logits(first, last):
                    w = slots(first, last, 0)
                    return v.tensor_tensor(w, w, logit_bias[:, None, :].broadcast_to([P, last - first, D]), ALU.add)

                def weighted(first, last):
                    w = slots(first, last, 1)
                    return v.tensor_tensor(w, w, slots(first, last, 0), ALU.mult)

                def max_of(b):
                    dve.wait_ge(lead_landed[b], 16 * LEAD * (k // 2) + 16 * LEAD)
                    fold_max(0, LEAD)

                    def more(quads):
                        for _ in range(quads - 1):
                            dve.reg_add(landed[b], landed[b], 16 * 4)
                        dve.wait_ge(rest_landed[b], landed[b])
                        fold_max(LEAD, LEAD + 4 * quads)
                        dve.reg_add(landed[b], landed[b], 16 * 4)
                    rest_of_block(dve, left, lambda: more(2), lambda: more(1), lambda: None)
                with dve.If(buf < 1):
                    max_of(0)
                with dve.Else():
                    max_of(1)
                new, old = flat(msg_max[:, bass.ds(buf, 1), :]), flat(msg_max[:, bass.ds(other, 1), :])
                then(v.tensor_tensor(new, run_max[:], neib, ALU.add))
                v.tensor_tensor(flat(rescale[:, bass.ds(buf, 1), :]), old, new, ALU.subtract).then_inc(scale_ready, 1)
                then(v.tensor_tensor(logit_bias[:], neib, new, ALU.subtract))
                logits(0, LEAD).then_inc(lead_ready, 1)
                rest_of_block(dve, left, lambda: logits(LEAD, SLOTS).then_inc(rest_ready, 1),
                              lambda: logits(LEAD, LEAD + 4).then_inc(rest_ready, 1), lambda: dve.drain().then_inc(rest_ready, 1))
                dve.wait_ge(lead_exp, k + 1)
                weighted(0, LEAD).then_inc(lead_weighted, 1)
                dve.wait_ge(rest_exp, k + 1)
                dve.sem_inc(passed, 1)
                rest_of_block(dve, left, lambda: weighted(LEAD, SLOTS).then_inc(rest_weighted, 1),
                              lambda: weighted(LEAD, LEAD + 4).then_inc(rest_weighted, 1), lambda: dve.drain().then_inc(rest_weighted, 1))
                with dve.If(k > 0):
                    fold_in(k, other)
                    with dve.If(j < 1):
                        then(finish_tile(nc.s_assert_within(t - 1, 0, NT - 1, skip_runtime_bounds_check_because="k > 0 and j < 1: not the first tile")))
            attention_blocks(dve, start_tile, softmax_block)
            end = dve.snap(dve.value_load(tile_row[0:1, 4 * NT - 2:4 * NT - 1], min_val=0, max_val=MAX_BLOCKS)
                           + dve.value_load(tile_row[0:1, 4 * NT - 4:4 * NT - 3], min_val=1, max_val=MAX_BLOCKS))
            fold_in(end, dve.snap((end + 1) % 2))
            finish_tile(NT - 1)

        @block.tensor
        def _(pe):
            m = nc.tensor
            pe.wait_ge(consts_made, 1)
            pe.wait_ge(rows_made, 1)
            for i in range(2 * CG):
                if i >= 4:
                    pe.wait_ge(cols_copied, i - 3)
                m.transpose(bank[i % 4][:, 0:P], (row_n, local_n)[i % 2][:, i // 2, :], ident[:]).then_inc(cols_transposed, 1)

            def transpose_h(b, n):
                pe.wait_ge(h_made, n + 1)
                for k in range(K):
                    last = m.transpose(ps_T[b][:, k * P:(k + 1) * P], h_tile[:, b, k * P:(k + 1) * P], ident[:])
                last.then_inc(h_transposed, 1)

            def messages(t, b, layer):
                n = layer * NT + t
                pe.wait_ge(hT_made, n + 3)
                for gr in range(G):
                    pe.wait_ge(evacuated, G * n + gr + 1)
                    m.matmul(ps_mm[gr].rearrange("p (r d) -> p r d", d=D), ones3[:],
                             bias3[:, layer:layer + 1, :].broadcast_to([3, 512 // D, D]), start=True, stop=False)
                    for k in range(K):
                        last = m.matmul(ps_mm[gr], hT[:, b, k, :], weights[layer][:, k, gr * 512:(gr + 1) * 512],
                                        start=False, stop=(k == K - 1))
                    last.then_inc(mm_done, 1)

            def layer1_input(t, b):
                pe.wait_ge(hT_made, t + 1)
                transpose_h(b, t)

            pe.wait_ge(cols_copied, 2 * CG)
            pe.wait_ge(weights_loaded, 16 * 2 * K)
            pe.wait_ge(bias3_loaded, 48)
            node_tiles_ahead(pe, layer1_input, lambda t, b: messages(t, b, 0))

            pe.wait_ge(rank_cols_made, 1)
            m.transpose(ps_prep[0:NT, 0:P], rank_deg[:], ident[:]).then_inc(deg_transposed, 1)
            pe.wait_ge(tiles_made, 1)
            m.matmul(ps_prep[0:NT, P:P + 1], before[:], tile_f[:], start=True, stop=True).then_inc(tile_prefix, 1)
            pe.wait_ge(att_w_loaded, 64)
            pe.wait_ge(evacuated, G * (NT + 1))
            for i in range(2):
                for ko in range(K):
                    for k in range(K):
                        last = m.transpose(ps_mm[2 * i + ko][:, k * P:(k + 1) * P], w_att_n[:, i, ko, k * P:(k + 1) * P], ident[:])
            last.then_inc(att_w_transposed, 1)

            def multiply(layer):
                with pe.Fori(0, ITERS) as i:
                    for half in range(2):
                        h = layer * HALVES + 2 * i + half
                        pe.wait_ge(onehot_ready, h + 1)
                        pe.wait_ge(half_added, h + 1)
                        pe.wait_ge(rows_landed[half], 16 * HALF * (layer * ITERS + i + 1))
                        for j in range(HALF):
                            for k in range(K):
                                col = (j * K + k) * WIN
                                last = m.matmul(ps_prod[half][:, col:col + WIN], ring[:, half, j, k * P:(k + 1) * P],
                                                onehot[:, half, j, :], start=True, stop=True)
                        last.then_inc(half_multiplied, 1)
            multiply(0)
            pe.wait_ge(att_w_made, 1)
            node_tiles(pe, lambda t, b: messages(t, b, 1))
            multiply(1)

            def turn_acc(t, b):
                pe.wait_ge(acc_copied, t + 1)
                pe.wait_ge(x_added, t + 1)
                for k in range(K):
                    last = m.transpose(ps_T[b][:, k * P:(k + 1) * P], hT[:, b, k, :], ident[:])
                last.then_inc(acc_transposed, 1)
            node_tiles(pe, turn_acc)

            def node_products(t, b):
                pe.wait_ge(hT_made, 2 * NT + t + 1)
                transpose_h(b, NT + t)
                pe.wait_ge(hT_made, 2 * NT + t + 3)
                pe.wait_ge(node_out_made, t + 1)
                for k in range(K):
                    last = m.matmul(ps_mm[b], hT[:, b, k, :], w_att[:, k, :, :], start=(k == 0), stop=(k == K - 1))
                last.then_inc(node_mm_done, 1)
            node_tiles(pe, node_products)

            pe.wait_ge(tile_row_loaded, 16)

            def sum_slots(t, j, k, left):
                buf = pe.snap(k % 2)

                def add(first, last_slot, closes):
                    for slot in range(first, last_slot):
                        last = m.matmul(flat(at_psum[:, bass.ds(buf, 1), :]), ident[:],
                                        at_ring[:, bass.ds(buf, 1), slot:slot + 1, :].rearrange("p b j c -> p (b j c)"),
                                        start=(slot == 0), stop=(closes and slot == last_slot - 1))
                        if closes and last_slot == LEAD and slot == LEAD - 2:
                            last.then_inc(rest_summed, 1)
                    return last

                def all_of(slots):
                    add(0, LEAD, False).then_inc(lead_summed, 1)
                    pe.wait_ge(rest_weighted, k + 1)
                    add(LEAD, slots, True).then_inc(rest_summed, 1)
                pe.wait_ge(lead_weighted, k + 1)
                pe.wait_ge(block_folded, k + 1)
                pe.sem_inc(passed, 1)
                rest_of_block(pe, left, lambda: all_of(SLOTS), lambda: all_of(LEAD + 4),
                              lambda: add(0, LEAD, True).then_inc(lead_summed, 1))
            attention_blocks(pe, lambda t: None, sum_slots)


def kernel(**inputs):
    import concourse.bacc as bacc
    from concourse.bass_utils import run_bass_kernel_spmd

    a = {name: np.ascontiguousarray(v) for name, v in inputs.items()}
    (n, d), (r, _, _), (e,) = a["x"].shape, a["L0_gnn_W0"].shape, a["dst"].shape
    s = Shapes(n, d, r, e)
    for name, pad in (("src", n), ("dst", PAD_DST), ("edge_type_8", 0)):
        a[name] = np.pad(a[name], (0, s.EP - e), constant_values=pad)
    nc = bacc.Bacc("TRN2", target_bir_lowering=False, num_devices=1)
    names = ("x", "src", "dst", "edge_type_8", "L0_gnn_W0", "L0_gnn_b0", "L0_gnn_W1", "L0_gnn_b1",
             "L1_gnn_W_nb", "L1_gnn_b_nb", "L1_gnn_W_self", "L1_gnn_b_self")
    args = [nc.dram_tensor(name, a[name].shape, mybir.dt.from_np(a[name].dtype), kind="ExternalInput").ap() for name in names]
    out = nc.dram_tensor("out", (n, d), mybir.dt.float32, kind="ExternalOutput").ap()
    gnn_kernel(nc, s, *args, out)
    r = run_bass_kernel_spmd(nc, [{name: a[name] for name in names}], core_ids=[0])
    return r.results[0]["out"]
```
